# Optimizing a Trainium2 kernel written in Bass

```python
import numpy as np
import jax
import jax.numpy as jnp

def _softmax(x, axis=-1):
    return jax.nn.softmax(x, axis=axis)

def _gelu(x):
    return jax.nn.gelu(x, approximate=True)

def _silu(x):
    return jax.nn.silu(x)

def _sigmoid(x):
    return jax.nn.sigmoid(x)

def _layernorm(x, axis=-1, eps=1e-05):
    m = jnp.mean(x, axis=axis, keepdims=True)
    v = jnp.var(x, axis=axis, keepdims=True)
    return (x - m) / jnp.sqrt(v + eps)

def _scatter_add(tgt, idx, src, axis=0):
    return tgt.at[idx].add(src)

def _segment_sum(src, seg, n):
    return jax.ops.segment_sum(src, seg, n)
kernel_name = 'mk_adj_resnorm_d1_adj_r2_edb933'

def setup_inputs(seed: int=0):
    np.random.seed(seed)
    _w = jnp.asarray

    def _rec_inputs():
        import jax
        import jax.numpy as jnp
        _gk = jax.random.key(seed)
        x = 7.22e-05 + 1 * jax.random.normal(jax.random.fold_in(_gk, 1), (32, 256, 512), jnp.float32)
        _w = (1.0 + jnp.arange(256, dtype=jnp.float32)) ** (-0.5)
        _w = _w / _w.mean()
        _pij = jnp.clip(0.015625 * _w[:, None] * _w[None, :], 0.0, 1.0)
        _a = jax.random.uniform(jax.random.fold_in(_gk, 2), (256, 256)) < _pij
        _a = jnp.logical_or(_a, jnp.eye(256, dtype=bool))
        _af = _a.astype(jnp.float32)
        adj = _af
        return (x, adj)
    x, adj = _rec_inputs()

    def _L0_gnn_setup():
        import jax, jax.numpy as jnp
        import numpy as np
        EPS = 1e-08

        def _row_stochastic_causal(A, causal_mask):
            A = A * causal_mask
            deg = jnp.maximum(A.sum(axis=-1, keepdims=True), EPS)
            return A / deg
        key = jax.random.key(seed)
        k = jax.random.split(key, 5)
        B, N, D = (4, 1024, 512)
        s = 1.0 / np.sqrt(D)
        h = jax.random.normal(k[0], (B, N, D), dtype=jnp.float32)
        W_lang = jax.random.normal(k[1], (D, D), dtype=jnp.float32) * s
        W_grav = jax.random.normal(k[2], (D, D), dtype=jnp.float32) * s
        W_V = jax.random.normal(k[3], (D, D), dtype=jnp.float32) * s
        W_O = jax.random.normal(k[4], (D, D), dtype=jnp.float32) * s
        causal_mask = jnp.tril(jnp.ones((N, N), dtype=jnp.float32))
        gate_logit = jnp.zeros((), jnp.float32)
        log_sigma = jnp.zeros((), jnp.float32)
        return {'h': h, 'causal_mask': causal_mask, 'W_lang': W_lang, 'W_grav': W_grav, 'W_V': W_V, 'W_O': W_O, 'gate_logit': gate_logit, 'log_sigma': log_sigma}
    _L0_gnn_all = _L0_gnn_setup()
    _L0_gnn_in = {k: v for k, v in _L0_gnn_all.items() if k in ('W_lang', 'W_grav', 'W_V', 'W_O', 'gate_logit', 'log_sigma')}
    del _L0_gnn_all
    return {'x': x, 'adj': adj, 'L0_gnn_W_lang': _L0_gnn_in['W_lang'], 'L0_gnn_W_grav': _L0_gnn_in['W_grav'], 'L0_gnn_W_V': _L0_gnn_in['W_V'], 'L0_gnn_W_O': _L0_gnn_in['W_O'], 'L0_gnn_gate_logit': _L0_gnn_in['gate_logit'], 'L0_gnn_log_sigma': _L0_gnn_in['log_sigma']}

def reference(x, adj, L0_gnn_W_lang, L0_gnn_W_grav, L0_gnn_W_V, L0_gnn_W_O, L0_gnn_gate_logit, L0_gnn_log_sigma):
    import jax
    import jax.numpy as jnp

    def _L0_gnn_ref(h, causal_mask, W_lang, W_grav, W_V, W_O, gate_logit, log_sigma):
        import jax, jax.numpy as jnp
        import numpy as np
        EPS = 1e-08

        def _row_stochastic_causal(A, causal_mask):
            A = A * causal_mask
            deg = jnp.maximum(A.sum(axis=-1, keepdims=True), EPS)
            return A / deg
        z_l = jnp.einsum('bnd,ed->bne', h, W_lang)
        z_g = jnp.einsum('bnd,ed->bne', h, W_grav)
        v = jnp.einsum('bnd,ed->bne', h, W_V)
        N = h.shape[-2]
        not_eye = 1.0 - jnp.eye(N, dtype=h.dtype)
        zn = z_l / jnp.maximum(jnp.linalg.norm(z_l, axis=-1, keepdims=True), EPS)
        A_l = jnp.maximum(jnp.einsum('bnd,bmd->bnm', zn, zn), 0.0) * not_eye
        sq = jnp.sum(z_g * z_g, axis=-1, keepdims=True)
        d2 = jnp.maximum(sq + jnp.swapaxes(sq, -1, -2) - 2.0 * jnp.einsum('bnd,bmd->bnm', z_g, z_g), 0.0)
        sigma = jnp.exp(log_sigma)
        A_g = jnp.exp(-d2 / (2.0 * sigma * sigma)) * not_eye
        K_l = _row_stochastic_causal(A_l, causal_mask)
        K_g = _row_stochastic_causal(A_g, causal_mask)
        w_l = jax.nn.sigmoid(gate_logit)
        K = w_l * K_l + (1.0 - w_l) * K_g
        out = jnp.einsum('bnm,bmd->bnd', K, v)
        return jnp.einsum('bnd,ed->bne', out, W_O)
    x = _layernorm(x + _L0_gnn_ref(x, adj, L0_gnn_W_lang, L0_gnn_W_grav, L0_gnn_W_V, L0_gnn_W_O, L0_gnn_gate_logit, L0_gnn_log_sigma), axis=-1)
    return x

_drawn_inputs = setup_inputs


def setup_inputs(seed=0):
    import zlib

    import numpy as np

    out = dict(_drawn_inputs(seed))
    spreads = {}
    factors = {}
    for name, (base, spread) in spreads.items():
        noise = np.random.default_rng([zlib.crc32(name.encode()), seed]).standard_normal(out[name].shape)
        drawn = base * np.exp(spread * noise) if base else spread * noise
        out[name] = jnp.asarray(drawn.astype(out[name].dtype))
    for name, factor in factors.items():
        out[name] = (out[name] * factor).astype(out[name].dtype)
    return out
```

```python
from contextlib import ExitStack

import concourse.bass as bass
from concourse import mybir

F32 = mybir.dt.float32
F32R = mybir.dt.float32r
ALU = mybir.AluOpType
ACT = mybir.ActivationFunctionType

EPS = 1e-8
LN_EPS = 1e-5
P = 128
L, G = 0, 1


def gnn_resnorm(nc, x, adj, w_lang, w_grav, w_v, w_o, gate_logit, log_sigma, out):
    B, N, D = x.shape
    NT, DT = N // P, D // P
    assert N == 256 and D == 512 and B % 4 == 0
    PAIRS = B // 2
    WIDE = 2 * N

    x_v = x.rearrange("b (t p) d -> b p t d", p=P)
    out_v = out.rearrange("b (t p) d -> b p t d", p=P)

    def upto(pair, per_pair, k):
        return pair * per_pair + k

    with ExitStack() as ctx:
        def sb(name, shape, dt=F32):
            return ctx.enter_context(nc.sbuf_tensor(name, shape, dt))

        def sem(name):
            return ctx.enter_context(nc.semaphore(name))

        x_nat = [sb(f"x_nat{i}", [P, 2, NT, D]) for i in range(2)]
        hT_hi = [sb(f"hT_hi{i}", [P, DT, 2, N], F32R) for i in range(2)]
        hT_lo = [sb(f"hT_lo{i}", [P, DT, 2, N], F32R) for i in range(2)]
        p_hi = sb("p_hi", [P, 2, DT, 2, N], F32R)
        p_lo = sb("p_lo", [P, 2, DT, 2, N], F32R)
        v_hi = sb("v_hi", [P, 2, NT, D], F32R)
        v_lo = sb("v_lo", [P, 2, NT, D], F32R)
        m_hi = sb("m_hi", [P, 2, DT, D], F32R)
        m_lo = sb("m_lo", [P, 2, DT, D], F32R)
        md_hi = sb("md_hi", [P, 2, DT, P], F32R)
        wvo_hi = sb("wvo_hi", [P, DT, D], F32R)
        wvo_lo = sb("wvo_lo", [P, DT, D], F32R)
        xs = sb("xs", [P, 2, NT, 2, N])
        work = sb("work", [P, 2, 6, WIDE])
        kt_hi = sb("kt_hi", [P, NT, N], F32R)
        kt_lo = sb("kt_lo", [P, NT, N], F32R)
        y = sb("y", [P, 2, NT, D])
        adj_off = sb("adj_off", [P, NT, N])
        ident = sb("ident", [P, P])
        ones = sb("ones", [P, P])
        junk_d = sb("junk_d", [P, 2, NT, P])
        junk_a = sb("junk_a", [P, NT, D])
        r_wide = sb("r_wide", [P, 2, NT, P])
        x_diag = sb("x_diag", [P, 2, 2, NT])
        norm2 = sb("norm2", [P, 2, NT])
        norm = sb("norm", [P, 2, NT])
        rnorm = sb("rnorm", [P, 2, NT])
        floor = sb("floor", [P, 2, 2, NT])
        sums = sb("sums", [P, 2, 2, NT])
        den = sb("den", [P, 2, 2, NT])
        rden = sb("rden", [P, 2, 2, NT])
        coef = sb("coef", [P, 2, 2, NT])
        share = sb("share", [P, 2, NT])
        half = sb("half", [P, NT])
        minus_half = sb("minus_half", [P, NT])
        one_by_d = sb("one_by_d", [P, NT])
        minus_one_by_d = sb("minus_one_by_d", [P, NT])
        eps_row = sb("eps_row", [P, NT])
        ln_eps_row = sb("ln_eps_row", [P, NT])
        msq = sb("msq", [P, 2, NT])
        shift = sb("shift", [P, 2, NT])
        row_sum = sb("row_sum", [P, 2, NT])
        minus_mean = sb("minus_mean", [P, 2, NT])
        row_sq = sb("row_sq", [P, 2, NT])
        var = sb("var", [P, 2, NT])
        rstd = sb("rstd", [P, 2, NT])
        scal = sb("scal", [P, 8])

        GL, SG, E, RADJ, BL, BG = range(6)
        K, GK = GL, E

        def wk(b, what):
            return work[:, b, what, :]

        def wk_t(b, what):
            return work[:, b, what, :].rearrange("p (t n) -> p t n", t=NT)

        CONSTANTS = ((ones, 1.0), (half, 0.5), (minus_half, -0.5), (floor, EPS), (one_by_d, 1.0 / D),
                     (minus_one_by_d, -1.0 / D), (eps_row, EPS), (ln_eps_row, LN_EPS))

        flat = work[:].rearrange("p b k d -> p (b k) d")
        raw = [flat[:, DT * i:DT * (i + 1)] for i in range(3)] + [y[:].rearrange("p b t d -> p (b t) d")]
        w_parts = {}
        for g in (L, G):
            w_parts[g] = tuple(t[:, g].rearrange("p k g n -> p k (g n)") for t in (p_hi, p_lo))
        w_parts[2] = tuple(t[:].rearrange("p b t d -> p (b t) d") for t in (v_hi, v_lo))
        woT = tuple(t[:].rearrange("p k b n -> p k (b n)") for t in (hT_hi[1], hT_lo[1]))

        bank = [ctx.enter_context(nc.psum_tensor(f"bank{i}", [P, WIDE], F32)) for i in range(8)]
        proj_bank = bank[0:3]
        turn_bank = bank[3]
        x_bank = bank[4:6]
        gl_bank = bank[6]
        gg_bank = bank[7]

        x_loaded = [[sem(f"x_loaded{parity}{b}") for b in range(2)] for parity in range(2)]
        w_loaded = [sem(f"w_loaded{i}") for i in range(3)]
        adj_loaded = sem("adj_loaded")
        scal_loaded = sem("scal_loaded")
        y_moved = [sem(f"y_moved{b}") for b in range(2)]
        zeroed = sem("zeroed")
        ident_ready = sem("ident_ready")
        consts_ready = sem("consts_ready")
        adj_ready = sem("adj_ready")
        scal_exp = sem("scal_exp")
        scal_steps = sem("scal_steps")
        w_hi_ready = sem("w_hi_ready")
        w_lo_ready = sem("w_lo_ready")
        prep_done = sem("prep_done")
        prep_hi = sem("prep_hi")
        prep_lo = sem("prep_lo")
        turned = sem("turned")
        hT_hi_ready = sem("hT_hi_ready")
        hT_ready = sem("hT_ready")
        proj_done = sem("proj_done")
        proj_hi = sem("proj_hi")
        proj_ready = sem("proj_ready")
        x_done = sem("x_done")
        x_saved = sem("x_saved")
        diag_ready = sem("diag_ready")
        centred = sem("centred")
        norm2_ready = sem("norm2_ready")
        r_ready = sem("r_ready")
        pool_steps = sem("pool_steps")
        gramT_done = sem("gramT_done")
        gram_ready = sem("gram_ready")
        rcol_done = sem("rcol_done")
        radj_ready = sem("radj_ready")
        exp_done = sem("exp_done")
        sums_ready = sem("sums_ready")
        coef_steps = sem("coef_steps")
        gk_ready = sem("gk_ready")
        k_ready = sem("k_ready")
        kt_done = sem("kt_done")
        kt_hi_ready = sem("kt_hi_ready")
        kt_ready = sem("kt_ready")
        out_done = sem("out_done")
        y_ready = sem("y_ready")
        mean_ready = sem("mean_ready")
        sq_ready = sem("sq_ready")
        ln_steps = sem("ln_steps")
        ln_ready = sem("ln_ready")
        normed = sem("normed")

        block = ctx.enter_context(nc.Block())
        PREP = 4 * DT
        PV = 2 * DT + 2 * NT
        LOOPS = (PAIRS - 2) // 2

        @block.sync
        def _(sp):
            def load_x(pair, parity, b):
                sp.dma_start(x_nat[parity][:, b], x_v[2 * pair + b]).then_inc(x_loaded[parity][b], 16)

            def store(pair, b):
                sp.wait_ge(normed, upto(pair, 4, 2 * b + 2))
                sp.dma_start(out_v[2 * pair + b], y[:, b]).then_inc(y_moved[b], 16)

            for b in range(2):
                load_x(0, 0, b)
            for b in range(2):
                load_x(1, 1, b)

            def pair(p, parity, last=False):
                for b in range(2):
                    if not last:
                        sp.wait_ge(y_ready, upto(p - 1, 4, 2 * b + 2))
                        load_x(p + 1, 1 - parity, b)
                    store(p - 1, b)

            with sp.Fori(0, LOOPS, 1) as i:
                pair(2 * i + 1, 1)
                pair(2 * i + 2, 0)
            pair(PAIRS - 1, 1, last=True)
            for b in range(2):
                store(PAIRS - 1, b)
            for b in range(2):
                sp.wait_ge(y_moved[b], 16 * (PAIRS + 1))

        @block.gpsimd
        def _(pool):
            nc.gpsimd.memset(ident[:], 0.0).then_inc(zeroed, 1)
            pool.wait_ge(zeroed, 1)
            nc.gpsimd.affine_select(out=ident[:], in_=ident[:], compare_op=ALU.not_equal, fill=1.0, base=0,
                                    pattern=[[-1, P]], channel_multiplier=1).then_inc(ident_ready, 1)
            for tile, value in CONSTANTS:
                nc.gpsimd.memset(tile[:], value).then_inc(consts_ready, 1)
            pool.wait_ge(adj_loaded, 16)
            for t in range(NT):
                nc.gpsimd.affine_select(out=adj_off[:, t], in_=adj_off[:, t], compare_op=ALU.not_equal, fill=0.0,
                                        base=t * P, pattern=[[-1, N]], channel_multiplier=1).then_inc(adj_ready, 1)

            def norms(p, b):
                done = upto(p, 6, 3 * b)
                pool.wait_ge(norm2_ready, upto(p, 2, b + 1))
                nc.gpsimd.tensor_tensor(rnorm[:, b], norm2[:, b], minus_half[:], ALU.pow).then_inc(pool_steps, 1)
                nc.gpsimd.tensor_tensor(norm[:, b], norm2[:, b], half[:], ALU.pow).then_inc(pool_steps, 1)
                pool.wait_ge(pool_steps, done + 1)
                for t in range(NT):
                    nc.gpsimd.tensor_tensor(r_wide[:, b, t], ones[:], rnorm[:, b, t:t + 1].broadcast_to([P, P]),
                                            ALU.mult).then_inc(r_ready, 1)
                pool.wait_ge(pool_steps, done + 2)
                nc.gpsimd.tensor_tensor(floor[:, b, L], norm[:, b], eps_row[:], ALU.mult).then_inc(pool_steps, 1)

            def layer_norm(q, b):
                done = upto(q, 6, 3 * b)
                pool.wait_ge(y_ready, upto(q, 4, 2 * b + 2))
                nc.gpsimd.tensor_tensor(minus_mean[:, b], row_sum[:, b], minus_one_by_d[:],
                                        ALU.mult).then_inc(mean_ready, 1)
                pool.wait_ge(sq_ready, upto(q, 4, 2 * b + 2))
                nc.gpsimd.tensor_tensor(msq[:, b], row_sq[:, b], one_by_d[:], ALU.mult).then_inc(ln_steps, 1)
                pool.wait_ge(ln_steps, done + 1)
                nc.gpsimd.tensor_tensor(var[:, b], msq[:, b], ln_eps_row[:], ALU.add).then_inc(ln_steps, 1)
                pool.wait_ge(ln_steps, done + 2)
                nc.gpsimd.tensor_tensor(rstd[:, b], var[:, b], minus_half[:], ALU.pow).then_inc(ln_steps, 1)
                pool.wait_ge(ln_steps, done + 3)
                nc.gpsimd.tensor_tensor(shift[:, b], minus_mean[:, b], rstd[:, b], ALU.mult).then_inc(ln_ready, 1)

            pool.wait_ge(consts_ready, len(CONSTANTS))
            for b in range(2):
                norms(0, b)

            def pair(p):
                for b in range(2):
                    layer_norm(p - 1, b)
                for b in range(2):
                    norms(p, b)

            with pool.Fori(1, PAIRS, 1) as p:
                pair(p)
            for b in range(2):
                layer_norm(PAIRS - 1, b)

        @block.scalar
        def _(act):
            for i, w in enumerate((w_lang, w_grav, w_v)):
                act.dma_start(raw[i], w.rearrange("(k p) d -> p k d", p=P)).then_inc(w_loaded[i], 16)
            for b in range(2):
                act.dma_start(y[:, b], w_o.rearrange("(b k p) d -> b p k d", b=2, p=P)[b]).then_inc(y_moved[b], 16)
            act.dma_start(adj_off[:], adj.rearrange("(t p) m -> p t m", p=P)).then_inc(adj_loaded, 16)
            act.dma_start(scal[:, 0:1], gate_logit.partition_broadcast(P)).then_inc(scal_loaded, 16)
            act.dma_start(scal[:, 1:2], log_sigma.partition_broadcast(P)).then_inc(scal_loaded, 16)

            def turn_hi(p, parity, b, k):
                act.wait_ge(turned, upto(p, 4, 2 * b + k + 1))
                nc.scalar.copy(hT_hi[parity][:, 2 * k:2 * k + 2, b, :],
                               turn_bank[:].rearrange("p (k n) -> p k n", k=2)).then_inc(hT_hi_ready, 1)

            for b in range(2):
                for k in range(2):
                    turn_hi(0, 0, b, k)
            for i in range(3):
                act.wait_ge(w_loaded[i], 16)
                nc.scalar.copy(w_parts[i][0], raw[i]).then_inc(w_hi_ready, 1)
            act.wait_ge(scal_loaded, 32)
            nc.scalar.activation(scal[:, 2:3], scal[:, 0:1], ACT.Exp, scale=-1.0).then_inc(scal_exp, 1)
            nc.scalar.activation(scal[:, 3:4], scal[:, 1:2], ACT.Exp).then_inc(scal_exp, 1)
            for u in range(PREP):
                g, i = divmod(u, DT)
                src = proj_bank[u % 3]
                act.wait_ge(prep_done, u + 1)
                if g < 2:
                    nc.scalar.copy(m_hi[:, g, i], src[:])
                    nc.scalar.mul(md_hi[:, g, i], src[:, i * P:(i + 1) * P], 0.5).then_inc(prep_hi, 1)
                else:
                    dst = woT[0][:, i] if g == 2 else wvo_hi[:, i]
                    nc.scalar.copy(dst, src[:]).then_inc(prep_hi, 1)

            def proj_hi_part(p, k):
                act.wait_ge(proj_done, upto(p, PV, k + 1))
                src = proj_bank[k % 3]
                if k < 2 * DT:
                    dst = p_hi[:, :, k // 2, k % 2, :]
                    src = src[:].rearrange("p (b n) -> p b n", b=2)
                else:
                    b, t = divmod(k - 2 * DT, NT)
                    dst, src = v_hi[:, b, t], src[:]
                nc.scalar.copy(dst, src).then_inc(proj_hi, 1)

            def save_x(p, b, t):
                act.wait_ge(x_done, upto(p, 4, 2 * b + t + 1))
                nc.scalar.copy(xs[:, b, t], x_bank[t][:].rearrange("p (g n) -> p g n", g=2)).then_inc(x_saved, 1)

            def gauss(q, b):
                act.wait_ge(gram_ready, upto(q, 4, 2 * b + 2))
                nc.scalar.activation(wk(b, E), wk(b, SG), ACT.Exp, scale=scal[:, 6:7]).then_inc(exp_done, 1)

            def gauss_scaled(q, b):
                act.wait_ge(coef_steps, upto(q, 6, 3 * b + 3))
                for t in range(NT):
                    nc.scalar.activation(wk_t(b, GK)[:, t], wk_t(b, BG)[:, t], ACT.Copy,
                                         scale=coef[:, b, G, t:t + 1]).then_inc(gk_ready, 1)

            def kt_hi_part(q, b):
                act.wait_ge(kt_done, upto(q, 2, b + 1))
                nc.scalar.copy(kt_hi[:], gl_bank[:].rearrange("p (t n) -> p t n", t=NT)).then_inc(kt_hi_ready, 1)

            def squares(q, b):
                act.wait_ge(mean_ready, upto(q, 2, b + 1))
                for t in range(NT):
                    nc.scalar.activation(junk_a[:, t], y[:, b, t], ACT.Square, bias=minus_mean[:, b, t:t + 1],
                                         accum_out=row_sq[:, b, t:t + 1]).then_inc(sq_ready, 1)

            def normalise(q, b):
                act.wait_ge(ln_ready, upto(q, 2, b + 1))
                for t in range(NT):
                    nc.scalar.activation(y[:, b, t], y[:, b, t], ACT.Identity, bias=shift[:, b, t:t + 1],
                                         scale=rstd[:, b, t:t + 1]).then_inc(normed, 1)

            def pair(p, parity, first=False, last=False):
                if not first:
                    act.wait_ge(x_done, upto(p, 4, 0))
                tail = not first
                proj_hi_part(p, 0)
                proj_hi_part(p, 1)
                if tail:
                    gauss(p - 1, 0)
                proj_hi_part(p, 2)
                if tail:
                    gauss_scaled(p - 1, 0)
                proj_hi_part(p, 3)
                if tail:
                    gauss(p - 1, 1)
                proj_hi_part(p, 4)
                if tail:
                    kt_hi_part(p - 1, 0)
                    gauss_scaled(p - 1, 1)
                proj_hi_part(p, 5)
                if tail:
                    squares(p - 1, 0)
                proj_hi_part(p, 6)
                if tail:
                    kt_hi_part(p - 1, 1)
                    normalise(p - 1, 0)
                proj_hi_part(p, 7)
                for b in range(2):
                    for t in range(NT):
                        if b == 0 and t == 0 and tail:
                            act.wait_ge(out_done, upto(p, 4, 0))
                        proj_hi_part(p, 2 * DT + NT * b + t)
                        if b == 0 and t == 0 and tail:
                            squares(p - 1, 1)
                        if b == 0 and t == 1 and tail:
                            normalise(p - 1, 1)
                        if b == 1 and t == 1:
                            save_x(p, 1, 0)
                            save_x(p, 1, 1)
                        if not last:
                            turn_hi(p + 1, 1 - parity, b, t)
                    if b == 0:
                        save_x(p, 0, 0)
                        save_x(p, 0, 1)

            pair(0, 0, first=True)
            with act.Fori(0, LOOPS, 1) as i:
                pair(2 * i + 1, 1)
                pair(2 * i + 2, 0)
            pair(PAIRS - 1, 1, last=True)
            for b in range(2):
                gauss(PAIRS - 1, b)
                gauss_scaled(PAIRS - 1, b)
            for b in range(2):
                kt_hi_part(PAIRS - 1, b)
                squares(PAIRS - 1, b)
                normalise(PAIRS - 1, b)

        @block.vector
        def _(dve):
            def turn_lo(p, parity, b, k):
                dve.wait_ge(hT_hi_ready, upto(p, 4, 2 * b + k + 1))
                nc.vector.tensor_tensor(hT_lo[parity][:, 2 * k:2 * k + 2, b, :],
                                        turn_bank[:].rearrange("p (k n) -> p k n", k=2),
                                        hT_hi[parity][:, 2 * k:2 * k + 2, b, :].bitcast(F32),
                                        ALU.subtract).then_inc(hT_ready, 1)

            for b in range(2):
                for k in range(2):
                    turn_lo(0, 0, b, k)
            for i in range(3):
                dve.wait_ge(w_hi_ready, i + 1)
                nc.vector.tensor_tensor(w_parts[i][1], raw[i], w_parts[i][0].bitcast(F32),
                                        ALU.subtract).then_inc(w_lo_ready, 1)
            dve.wait_ge(scal_exp, 2)
            nc.vector.tensor_scalar(scal[:, 4:5], scal[:, 2:3], 1.0, None, ALU.add).then_inc(scal_steps, 1)
            nc.vector.tensor_tensor(scal[:, 5:6], scal[:, 3:4], scal[:, 3:4], ALU.mult).then_inc(scal_steps, 1)
            dve.wait_ge(scal_steps, 2)
            nc.vector.reciprocal(scal[:, 7:8], scal[:, 4:5]).then_inc(scal_steps, 1)
            nc.vector.reciprocal(scal[:, 6:7], scal[:, 5:6]).then_inc(scal_steps, 1)
            dve.wait_ge(scal_steps, 4)
            for t in range(NT):
                nc.vector.tensor_copy(share[:, L, t:t + 1], scal[:, 7:8]).then_inc(scal_steps, 1)
                nc.vector.tensor_scalar(share[:, G, t:t + 1], scal[:, 7:8], -1.0, 1.0, ALU.mult,
                                        ALU.add).then_inc(scal_steps, 1)
            for u in range(PREP):
                g, i = divmod(u, DT)
                src = proj_bank[u % 3]
                dve.wait_ge(prep_hi, u + 1)
                if g < 2:
                    a, e = i * P, (i + 1) * P
                    if e < D:
                        nc.vector.tensor_tensor(m_lo[:, g, i, e:], src[:, e:], m_hi[:, g, i, e:].bitcast(F32),
                                                ALU.subtract)
                    nc.vector.scalar_tensor_tensor(out=m_lo[:, g, i, a:e], in0=src[:, a:e], scalar=0.5,
                                                   in1=md_hi[:, g, i].bitcast(F32), op0=ALU.mult,
                                                   op1=ALU.subtract).then_inc(prep_lo, 1)
                else:
                    hi, lo = (woT[0][:, i], woT[1][:, i]) if g == 2 else (wvo_hi[:, i], wvo_lo[:, i])
                    nc.vector.tensor_tensor(lo, src[:], hi.bitcast(F32), ALU.subtract).then_inc(prep_lo, 1)

            def proj_lo_part(p, k):
                dve.wait_ge(proj_hi, upto(p, PV, k + 1))
                src = proj_bank[k % 3]
                if k < 2 * DT:
                    hi, dst = p_hi[:, :, k // 2, k % 2, :], p_lo[:, :, k // 2, k % 2, :]
                    src = src[:].rearrange("p (b n) -> p b n", b=2)
                else:
                    b, t = divmod(k - 2 * DT, NT)
                    hi, dst, src = v_hi[:, b, t], v_lo[:, b, t], src[:]
                nc.vector.tensor_tensor(dst, src, hi.bitcast(F32), ALU.subtract).then_inc(proj_ready, 1)

            def diagonal(p, b):
                dve.wait_ge(x_saved, upto(p, 4, 2 * b + 2))
                for g in (G, L):
                    for t in range(NT):
                        ins = nc.vector.tensor_tensor_reduce(
                            out=junk_d[:, g, t], in0=xs[:, b, t, g, t * P:(t + 1) * P], in1=ident[:], scale=1.0,
                            scalar=0.0, op0=ALU.mult, op1=ALU.add, accum_out=x_diag[:, b, g, t:t + 1])
                ins.then_inc(diag_ready, 1)
                dve.wait_ge(diag_ready, upto(p, 2, b + 1))
                nc.vector.tensor_scalar(norm2[:, b], x_diag[:, b, L], 2.0, EPS * EPS, ALU.mult,
                                        ALU.max).then_inc(norm2_ready, 1)
                for t in range(NT):
                    nc.vector.tensor_scalar(xs[:, b, t, G], xs[:, b, t, G], x_diag[:, b, G, t:t + 1], None,
                                            ALU.subtract).then_inc(centred, 1)

            def gram(q, b, g):
                dve.wait_ge(gramT_done, upto(q, 4, 2 * b + g + 1))
                src = (gl_bank, gg_bank)[g]
                nc.vector.tensor_tensor(wk_t(b, (GL, SG)[g]), src[:].rearrange("p (t n) -> p t n", t=NT),
                                        xs[:, b, :, g], ALU.add).then_inc(gram_ready, 1)

            def gauss_masked(q, b):
                dve.wait_ge(exp_done, upto(q, 2, b + 1))
                for t in range(NT):
                    nc.vector.scalar_tensor_tensor(
                        out=wk_t(b, BG)[:, t], in0=wk_t(b, E)[:, t], scalar=1.0, in1=adj_off[:, t], op0=ALU.min,
                        op1=ALU.mult, accum_out=sums[:, b, G, t:t + 1]).then_inc(sums_ready, 1)

            def cosine_masked(q, b):
                dve.wait_ge(rcol_done, upto(q, 2, b + 1))
                nc.vector.tensor_tensor(wk_t(b, RADJ), gg_bank[:, 0:N].unsqueeze(1).broadcast_to([P, NT, N]),
                                        adj_off[:], ALU.mult).then_inc(radj_ready, 1)
                dve.wait_ge(radj_ready, upto(q, 2, b + 1))
                for t in range(NT):
                    nc.vector.scalar_tensor_tensor(
                        out=wk_t(b, BL)[:, t], in0=wk_t(b, GL)[:, t], scalar=0.0, in1=wk_t(b, RADJ)[:, t],
                        op0=ALU.max, op1=ALU.mult, accum_out=sums[:, b, L, t:t + 1]).then_inc(sums_ready, 1)

            def row_factors(q, b):
                done = upto(q, 6, 3 * b)
                dve.wait_ge(sums_ready, upto(q, 8, 4 * b + 4))
                dve.wait_ge(pool_steps, upto(q, 6, 3 * b + 3))
                nc.vector.tensor_tensor(den[:, b], sums[:, b], floor[:, b], ALU.max).then_inc(coef_steps, 1)
                dve.wait_ge(coef_steps, done + 1)
                nc.vector.reciprocal(rden[:, b], den[:, b]).then_inc(coef_steps, 1)
                dve.wait_ge(coef_steps, done + 2)
                nc.vector.tensor_tensor(coef[:, b], rden[:, b], share[:], ALU.mult).then_inc(coef_steps, 1)

            def kernel_sum(q, b):
                dve.wait_ge(coef_steps, upto(q, 6, 3 * b + 3))
                for t in range(NT):
                    dve.wait_ge(gk_ready, upto(q, 4, 2 * b + t + 1))
                    nc.vector.scalar_tensor_tensor(
                        out=wk_t(b, K)[:, t], in0=wk_t(b, BL)[:, t], scalar=coef[:, b, L, t:t + 1],
                        in1=wk_t(b, GK)[:, t], op0=ALU.mult, op1=ALU.add).then_inc(k_ready, 1)

            def kt_lo_part(q, b):
                dve.wait_ge(kt_hi_ready, upto(q, 2, b + 1))
                nc.vector.tensor_tensor(kt_lo[:], gl_bank[:].rearrange("p (t n) -> p t n", t=NT),
                                        kt_hi[:].bitcast(F32), ALU.subtract).then_inc(kt_ready, 1)

            def residual(q, parity, b, t):
                dve.wait_ge(out_done, upto(q, 4, 2 * b + t + 1))
                nc.vector.scalar_tensor_tensor(
                    out=y[:, b, t], in0=turn_bank[:], scalar=1.0, in1=x_nat[parity][:, b, t], op0=ALU.mult,
                    op1=ALU.add, accum_out=row_sum[:, b, t:t + 1]).then_inc(y_ready, 1)

            def pair(p, parity, first=False, last=False):
                tail = not first
                q = p - 1
                proj_lo_part(p, 0)
                if tail:
                    gram(q, 0, L)
                    gram(q, 0, G)
                proj_lo_part(p, 1)
                if tail:
                    cosine_masked(q, 0)
                    gauss_masked(q, 0)
                    row_factors(q, 0)
                proj_lo_part(p, 2)
                if tail:
                    gram(q, 1, L)
                    gram(q, 1, G)
                    kernel_sum(q, 0)
                proj_lo_part(p, 3)
                if tail:
                    cosine_masked(q, 1)
                    gauss_masked(q, 1)
                    row_factors(q, 1)
                proj_lo_part(p, 4)
                if tail:
                    kt_lo_part(q, 0)
                    kernel_sum(q, 1)
                proj_lo_part(p, 5)
                if tail:
                    dve.wait_ge(y_moved[0], 16 * (q + 1))
                    residual(q, 1 - parity, 0, 0)
                    residual(q, 1 - parity, 0, 1)
                proj_lo_part(p, 6)
                if tail:
                    kt_lo_part(q, 1)
                proj_lo_part(p, 7)
                if tail:
                    dve.wait_ge(y_moved[1], 16 * (q + 1))
                    residual(q, 1 - parity, 1, 0)
                    residual(q, 1 - parity, 1, 1)
                for b in range(2):
                    for t in range(NT):
                        proj_lo_part(p, 2 * DT + NT * b + t)
                        if not last:
                            turn_lo(p + 1, 1 - parity, b, t)
                    diagonal(p, b)

            pair(0, 0, first=True)
            dve.wait_ge(adj_ready, NT)
            dve.wait_ge(scal_steps, 8)
            with dve.Fori(0, LOOPS, 1) as i:
                pair(2 * i + 1, 1)
                pair(2 * i + 2, 0)
            pair(PAIRS - 1, 1, last=True)
            q = PAIRS - 1
            for b in range(2):
                gram(q, b, L)
                gram(q, b, G)
                cosine_masked(q, b)
                gauss_masked(q, b)
                row_factors(q, b)
            for b in range(2):
                kernel_sum(q, b)
            for b in range(2):
                kt_lo_part(q, b)
                dve.wait_ge(y_moved[b], 16 * (q + 1))
                residual(q, 1, b, 0)
                residual(q, 1, b, 1)

        @block.tensor
        def _(pe):
            def products(dst, steps):
                for n, (lhsT, rhs) in enumerate(steps):
                    last = pe.matmul(dst, lhsT, rhs, start=(n == 0), stop=(n == len(steps) - 1))
                return last

            def turn(p, parity, b, k):
                n = upto(p, 4, 2 * b + k)
                if k == 0:
                    pe.wait_ge(x_loaded[parity][b], 8 * (p - parity) + 16)
                if b + k > 0:
                    pe.wait_ge(hT_ready, n)
                for kk in range(2):
                    for t in range(NT):
                        c = (2 * k + kk) * P
                        last = pe.transpose(turn_bank[:, kk * N + t * P:kk * N + (t + 1) * P],
                                            x_nat[parity][:, b, t, c:c + P], ident[:])
                last.then_inc(turned, 1)

            pe.wait_ge(ident_ready, 1)
            for b in range(2):
                for k in range(2):
                    turn(0, 0, b, k)

            for u in range(PREP):
                g, i = divmod(u, DT)
                dst = proj_bank[u % 3]
                if u >= 3:
                    pe.wait_ge(prep_lo, u - 2)
                rows = slice(i * P, (i + 1) * P)
                if g < 2:
                    pe.wait_ge(w_lo_ready, g + 1)
                    hi, lo = w_parts[g]
                    steps = [s for r in range(DT) for s in ((hi[:, r, rows], hi[:, r]), (hi[:, r, rows], lo[:, r]),
                                                            (lo[:, r, rows], hi[:, r]))]
                    products(dst[:], steps).then_inc(prep_done, 1)
                elif g == 2:
                    for b in range(2):
                        pe.wait_ge(y_moved[b], 16)
                    for r in range(DT):
                        last = pe.transpose(dst[:, r * P:(r + 1) * P], raw[3][:, r, rows], ident[:])
                    last.then_inc(prep_done, 1)
                else:
                    pe.wait_ge(w_lo_ready, 3)
                    pe.wait_ge(prep_lo, 3 * DT)
                    (vh, vl), (oh, ol) = w_parts[2], woT
                    steps = [s for r in range(DT) for s in ((vh[:, r, rows], oh[:, r]), (vh[:, r, rows], ol[:, r]),
                                                            (vl[:, r, rows], oh[:, r]))]
                    products(dst[:], steps).then_inc(prep_done, 1)

            def project(p, parity, k, first):
                j, g = divmod(k, 2)
                if k == 0:
                    pe.wait_ge(hT_ready, upto(p, 4, 4))
                if not (first and k < 3):
                    pe.wait_ge(proj_ready, upto(p, PV, k - 2))
                elif k == 0:
                    pe.wait_ge(prep_lo, PREP)
                hi = [hT_hi[parity][:, i].rearrange("p b n -> p (b n)") for i in range(DT)]
                lo = [hT_lo[parity][:, i].rearrange("p b n -> p (b n)") for i in range(DT)]
                c = slice(j * P, (j + 1) * P)
                steps = []
                for i in range(DT):
                    steps.append((m_hi[:, g, i, c], lo[i]))
                    if i <= j:
                        steps.append((m_hi[:, g, i, c] if i < j else md_hi[:, g, i], hi[i]))
                        steps.append((m_lo[:, g, i, c], hi[i]))
                products(proj_bank[k % 3][:], steps).then_inc(proj_done, 1)

            def value(p, parity, b, t):
                k = 2 * DT + NT * b + t
                pe.wait_ge(proj_ready, upto(p, PV, k - 2))
                rows = slice(t * P, (t + 1) * P)
                steps = []
                for i in range(DT):
                    hi, lo = hT_hi[parity][:, i, b, rows], hT_lo[parity][:, i, b, rows]
                    steps += [(hi, wvo_hi[:, i]), (hi, wvo_lo[:, i]), (lo, wvo_hi[:, i])]
                products(proj_bank[k % 3][:], steps).then_inc(proj_done, 1)

            def x_tile(p, parity, b, t):
                n = upto(p, 4, 2 * b + t)
                if b == 0 and t == 0:
                    pe.wait_ge(proj_ready, upto(p, PV, 2 * DT))
                if not (type(n) is int and n < 2):
                    pe.wait_ge(x_saved, n - 1)
                steps = []
                for i in range(DT):
                    lhsT = hT_hi[parity][:, i, b, t * P:(t + 1) * P]
                    steps += [(lhsT, part[:, b, i].rearrange("p g n -> p (g n)")) for part in (p_hi, p_lo)]
                products(x_bank[t][:], steps).then_inc(x_done, 1)

            def gram_turn(q, b, g):
                if g == L:
                    pe.wait_ge(x_saved, upto(q, 4, 2 * b + 2))
                else:
                    pe.wait_ge(centred, upto(q, 4, 2 * b + 2))
                if g == L and b == 1:
                    pe.wait_ge(gram_ready, upto(q, 4, 1))
                if g == G and b == 1:
                    pe.wait_ge(radj_ready, upto(q, 2, 1))
                dst = (gl_bank, gg_bank)[g]
                for t in range(NT):
                    for u in range(NT):
                        last = pe.transpose(dst[:, t * N + u * P:t * N + (u + 1) * P],
                                            xs[:, b, u, g, t * P:(t + 1) * P], ident[:])
                last.then_inc(gramT_done, 1)

            def r_turn(q, b):
                pe.wait_ge(r_ready, upto(q, 4, 2 * b + 2))
                pe.wait_ge(gram_ready, upto(q, 4, 2 * b + 2))
                for t in range(NT):
                    last = pe.transpose(gg_bank[:, t * P:(t + 1) * P], r_wide[:, b, t], ident[:])
                last.then_inc(rcol_done, 1)

            def k_turn(q, b):
                pe.wait_ge(k_ready, upto(q, 4, 2 * b + 2))
                if b == 0:
                    pe.wait_ge(gram_ready, upto(q, 4, 3))
                else:
                    pe.wait_ge(kt_ready, upto(q, 2, 1))
                for u in range(NT):
                    for t in range(NT):
                        last = pe.transpose(gl_bank[:, u * N + t * P:u * N + (t + 1) * P],
                                            wk_t(b, K)[:, t, u * P:(u + 1) * P], ident[:])
                last.then_inc(kt_done, 1)

            def k_times_v(q, b, t, bank_free, count):
                if t == 0:
                    pe.wait_ge(kt_ready, upto(q, 2, b + 1))
                pe.wait_ge(bank_free, count)
                steps = []
                for u in range(NT):
                    hi, lo = kt_hi[:, u, t * P:(t + 1) * P], kt_lo[:, u, t * P:(t + 1) * P]
                    steps += [(hi, v_hi[:, b, u]), (hi, v_lo[:, b, u]), (lo, v_hi[:, b, u])]
                products(turn_bank[:], steps).then_inc(out_done, 1)

            def outputs(q, b):
                for t in range(NT):
                    if b + t == 0:
                        k_times_v(q, b, t, hT_ready, upto(q + 1, 4, 4))
                    else:
                        k_times_v(q, b, t, y_ready, upto(q, 4, 2 * b + t))

            def pair(p, parity, first=False, last=False):
                tail = not first
                q = p - 1
                project(p, parity, 0, first)
                if tail:
                    gram_turn(q, 0, L)
                    gram_turn(q, 0, G)
                project(p, parity, 1, first)
                if tail:
                    r_turn(q, 0)
                project(p, parity, 2, first)
                if tail:
                    gram_turn(q, 1, L)
                    gram_turn(q, 1, G)
                project(p, parity, 3, first)
                if tail:
                    r_turn(q, 1)
                project(p, parity, 4, first)
                if tail:
                    k_turn(q, 0)
                project(p, parity, 5, first)
                if tail:
                    outputs(q, 0)
                project(p, parity, 6, first)
                if tail:
                    k_turn(q, 1)
                project(p, parity, 7, first)
                if tail:
                    outputs(q, 1)
                    if not last:
                        pe.wait_ge(y_ready, upto(q, 4, 4))
                for b in range(2):
                    for t in range(NT):
                        value(p, parity, b, t)
                        if b == 1 and t == 1:
                            x_tile(p, parity, 1, 0)
                            x_tile(p, parity, 1, 1)
                        if not last:
                            turn(p + 1, 1 - parity, b, t)
                    if b == 0:
                        x_tile(p, parity, 0, 0)
                        x_tile(p, parity, 0, 1)

            pair(0, 0, first=True)
            with pe.Fori(0, LOOPS, 1) as i:
                pair(2 * i + 1, 1)
                pair(2 * i + 2, 0)
            pair(PAIRS - 1, 1, last=True)
            q = PAIRS - 1
            for b in range(2):
                gram_turn(q, b, L)
                gram_turn(q, b, G)
                r_turn(q, b)
            for b in range(2):
                k_turn(q, b)
                for t in range(NT):
                    if b + t == 0:
                        k_times_v(q, b, t, y_ready, upto(q, 4, 0))
                    else:
                        k_times_v(q, b, t, y_ready, upto(q, 4, 2 * b + t))


_INS = ['x', 'adj', 'L0_gnn_W_lang', 'L0_gnn_W_grav', 'L0_gnn_W_V', 'L0_gnn_W_O', 'L0_gnn_gate_logit',
        'L0_gnn_log_sigma']


def kernel(**inputs):
    import numpy as _np
    import concourse.bacc as _bacc
    from concourse.bass_utils import run_bass_kernel_spmd as _run

    nc = _bacc.Bacc("TRN2", target_bir_lowering=False, num_devices=1)
    arrays, args = {}, []
    for name in _INS:
        a = _np.ascontiguousarray(inputs[name])
        arrays[f"in_{name}"] = a
        args.append(nc.dram_tensor(f"in_{name}", a.shape, mybir.dt.from_np(a.dtype), kind="ExternalInput").ap())
    out = nc.dram_tensor("out_y", arrays["in_x"].shape, F32, kind="ExternalOutput").ap()
    gnn_resnorm(nc, *args, out)
    r = _run(nc, [arrays], core_ids=[0])
    return r.results[0]["out_y"]
```

```python
from contextlib import ExitStack

import concourse.bass as bass
from concourse import mybir

F32 = mybir.dt.float32
F32R = mybir.dt.float32r
ALU = mybir.AluOpType
ACT = mybir.ActivationFunctionType

EPS = 1e-8
LN_EPS = 1e-5
P = 128
L, G = 0, 1


def gnn_resnorm(nc, x, adj, w_lang, w_grav, w_v, w_o, gate_logit, log_sigma, out):
    B, N, D = x.shape
    NT, DT = N // P, D // P
    assert N == 256 and D == 512 and B % 4 == 0
    PAIRS = B // 2
    WIDE = 2 * N

    x_v = x.rearrange("b (t p) d -> b p t d", p=P)
    out_v = out.rearrange("b (t p) d -> b p t d", p=P)

    def upto(pair, per_pair, k):
        return pair * per_pair + k

    with ExitStack() as ctx:
        def sb(name, shape, dt=F32):
            return ctx.enter_context(nc.sbuf_tensor(name, shape, dt))

        def sem(name):
            return ctx.enter_context(nc.semaphore(name))

        x_nat = [sb(f"x_nat{i}", [P, 2, NT, D]) for i in range(2)]
        hT_hi = [sb(f"hT_hi{i}", [P, DT, 2, N], F32R) for i in range(2)]
        hT_lo = [sb(f"hT_lo{i}", [P, DT, 2, N], F32R) for i in range(2)]
        p_hi = sb("p_hi", [P, 2, DT, 2, N], F32R)
        p_lo = sb("p_lo", [P, 2, DT, 2, N], F32R)
        v_hi = sb("v_hi", [P, 2, NT, D], F32R)
        v_lo = sb("v_lo", [P, 2, NT, D], F32R)
        m_hi = sb("m_hi", [P, 2, DT, D], F32R)
        m_lo = sb("m_lo", [P, 2, DT, D], F32R)
        md_hi = sb("md_hi", [P, 2, DT, P], F32R)
        wvo_hi = sb("wvo_hi", [P, DT, D], F32R)
        wvo_lo = sb("wvo_lo", [P, DT, D], F32R)
        xs = sb("xs", [P, 2, NT, 2, N])
        work = sb("work", [P, 2, 6, WIDE])
        kt_hi = sb("kt_hi", [P, NT, N], F32R)
        kt_lo = sb("kt_lo", [P, NT, N], F32R)
        y = sb("y", [P, 2, NT, D])
        adj_off = sb("adj_off", [P, NT, N])
        ident = sb("ident", [P, P])
        ones = sb("ones", [P, P])
        junk_d = sb("junk_d", [P, 2, NT, P])
        junk_a = sb("junk_a", [P, NT, D])
        r_wide = sb("r_wide", [P, 2, NT, P])
        x_diag = sb("x_diag", [P, 2, 2, NT])
        norm2 = sb("norm2", [P, 2, NT])
        norm = sb("norm", [P, 2, NT])
        rnorm = sb("rnorm", [P, 2, NT])
        floor = sb("floor", [P, 2, 2, NT])
        sums = sb("sums", [P, 2, 2, NT])
        den = sb("den", [P, 2, 2, NT])
        rden = sb("rden", [P, 2, 2, NT])
        coef = sb("coef", [P, 2, 2, NT])
        share = sb("share", [P, 2, NT])
        half = sb("half", [P, NT])
        minus_half = sb("minus_half", [P, NT])
        one_by_d = sb("one_by_d", [P, NT])
        minus_one_by_d = sb("minus_one_by_d", [P, NT])
        eps_row = sb("eps_row", [P, NT])
        ln_eps_row = sb("ln_eps_row", [P, NT])
        msq = sb("msq", [P, 2, NT])
        shift = sb("shift", [P, 2, NT])
        row_sum = sb("row_sum", [P, 2, NT])
        minus_mean = sb("minus_mean", [P, 2, NT])
        row_sq = sb("row_sq", [P, 2, NT])
        var = sb("var", [P, 2, NT])
        rstd = sb("rstd", [P, 2, NT])
        scal = sb("scal", [P, 8])

        GL, SG, E, RADJ, BL, BG = range(6)
        K, GK = GL, E

        def wk(b, what):
            return work[:, b, what, :]

        def wk_t(b, what):
            return work[:, b, what, :].rearrange("p (t n) -> p t n", t=NT)

        CONSTANTS = ((ones, 1.0), (half, 0.5), (minus_half, -0.5), (floor, EPS), (one_by_d, 1.0 / D),
                     (minus_one_by_d, -1.0 / D), (eps_row, EPS), (ln_eps_row, LN_EPS))

        flat = work[:].rearrange("p b k d -> p (b k) d")
        raw = [flat[:, DT * i:DT * (i + 1)] for i in range(3)] + [y[:].rearrange("p b t d -> p (b t) d")]
        w_parts = {}
        for g in (L, G):
            w_parts[g] = tuple(t[:, g].rearrange("p k g n -> p k (g n)") for t in (p_hi, p_lo))
        w_parts[2] = tuple(t[:].rearrange("p b t d -> p (b t) d") for t in (v_hi, v_lo))
        woT = tuple(t[:].rearrange("p k b n -> p k (b n)") for t in (hT_hi[1], hT_lo[1]))

        bank = [ctx.enter_context(nc.psum_tensor(f"bank{i}", [P, WIDE], F32)) for i in range(8)]
        proj_bank = bank[0:3]
        turn_bank = bank[3]
        x_bank = bank[4:6]
        gl_bank = bank[6]
        gg_bank = bank[7]

        x_loaded = [[sem(f"x_loaded{parity}{b}") for b in range(2)] for parity in range(2)]
        w_loaded = [[sem(f"w_loaded{i}{h}") for h in range(2)] for i in range(3)]
        adj_loaded = sem("adj_loaded")
        scal_loaded = sem("scal_loaded")
        y_moved = [sem(f"y_moved{b}") for b in range(2)]
        zeroed = sem("zeroed")
        ident_ready = sem("ident_ready")
        consts_ready = sem("consts_ready")
        adj_ready = sem("adj_ready")
        scal_exp = sem("scal_exp")
        scal_steps = sem("scal_steps")
        w_hi_ready = sem("w_hi_ready")
        w_lo_ready = sem("w_lo_ready")
        prep_done = sem("prep_done")
        prep_hi = sem("prep_hi")
        prep_lo = sem("prep_lo")
        turned = sem("turned")
        hT_hi_ready = sem("hT_hi_ready")
        hT_ready = sem("hT_ready")
        proj_done = sem("proj_done")
        proj_hi = sem("proj_hi")
        proj_ready = sem("proj_ready")
        x_done = sem("x_done")
        x_saved = sem("x_saved")
        diag_ready = sem("diag_ready")
        centred = sem("centred")
        norm2_ready = sem("norm2_ready")
        r_ready = sem("r_ready")
        pool_steps = sem("pool_steps")
        gramT_done = sem("gramT_done")
        gram_ready = sem("gram_ready")
        rcol_done = sem("rcol_done")
        radj_ready = sem("radj_ready")
        exp_done = sem("exp_done")
        sums_ready = sem("sums_ready")
        coef_steps = sem("coef_steps")
        gk_ready = sem("gk_ready")
        k_ready = sem("k_ready")
        kt_done = sem("kt_done")
        kt_hi_ready = sem("kt_hi_ready")
        kt_ready = sem("kt_ready")
        out_done = sem("out_done")
        y_ready = sem("y_ready")
        mean_ready = sem("mean_ready")
        sq_ready = sem("sq_ready")
        ln_steps = sem("ln_steps")
        ln_ready = sem("ln_ready")
        normed = sem("normed")

        block = ctx.enter_context(nc.Block())
        UPPER, MIRROR, WO_TURN, WVO = range(4)
        prep_units = [(UPPER, L, i) for i in range(DT)] + [(UPPER, G, 0)]
        for i in range(1, DT):
            prep_units += [(MIRROR, L, i), (UPPER, G, i)]
        BEFORE_TURNS = len(prep_units)
        prep_units += [(WO_TURN, None, i) for i in range(DT)] + [(WVO, None, 0)]
        for i in range(1, DT):
            prep_units += [(MIRROR, G, i), (WVO, None, i)]
        PREP = len(prep_units)

        def prepared(kind, g, i):
            return prep_units.index((kind, g, i)) + 1

        def upto_unit(u):
            return sum(kind != MIRROR for kind, _, _ in prep_units[:u + 1])

        def first_bank(b, k):
            return (x_bank[0], x_bank[1], gl_bank, turn_bank)[2 * b + k]

        def tail_bank(b, t):
            return (turn_bank, x_bank[0], x_bank[1], gg_bank)[2 * b + t]

        PV = 2 * DT + 2 * NT
        LOOPS = (PAIRS - 2) // 2

        def load_w(queue, i, w, h):
            queue.dma_start(raw[i][:, 2 * h:2 * h + 2],
                            w.rearrange("(h k p) d -> h p k d", h=2, p=P)[h]).then_inc(w_loaded[i][h], 16)

        @block.sync
        def _(sp):
            def load_x(pair, parity, b):
                sp.dma_start(x_nat[parity][:, b], x_v[2 * pair + b]).then_inc(x_loaded[parity][b], 16)

            def store(pair, b):
                sp.wait_ge(normed, upto(pair, 4, 2 * b + 2))
                sp.dma_start(out_v[2 * pair + b], y[:, b]).then_inc(y_moved[b], 16)

            load_w(sp, L, w_lang, 0)
            for h in range(2):
                load_w(sp, G, w_grav, h)
            for h in range(2):
                load_w(sp, 2, w_v, h)
            for b in range(2):
                load_x(0, 0, b)
            for b in range(2):
                sp.dma_start(y[:, b], w_o.rearrange("(b k p) d -> b p k d", b=2, p=P)[b]).then_inc(y_moved[b], 16)
            sp.dma_start(adj_off[:], adj.rearrange("(t p) m -> p t m", p=P)).then_inc(adj_loaded, 16)
            sp.dma_start(scal[:, 0:1], gate_logit.partition_broadcast(P)).then_inc(scal_loaded, 16)
            sp.dma_start(scal[:, 1:2], log_sigma.partition_broadcast(P)).then_inc(scal_loaded, 16)
            for b in range(2):
                load_x(1, 1, b)

            def pair(p, parity, last=False):
                for b in range(2):
                    if not last:
                        sp.wait_ge(y_ready, upto(p - 1, 4, 2 * b + 2))
                        load_x(p + 1, 1 - parity, b)
                    store(p - 1, b)

            with sp.Fori(0, LOOPS, 1) as i:
                pair(2 * i + 1, 1)
                pair(2 * i + 2, 0)
            pair(PAIRS - 1, 1, last=True)
            for b in range(2):
                store(PAIRS - 1, b)
            for b in range(2):
                sp.wait_ge(y_moved[b], 16 * (PAIRS + 1))

        @block.gpsimd
        def _(pool):
            nc.gpsimd.memset(ident[:], 0.0).then_inc(zeroed, 1)
            pool.wait_ge(zeroed, 1)
            nc.gpsimd.affine_select(out=ident[:], in_=ident[:], compare_op=ALU.not_equal, fill=1.0, base=0,
                                    pattern=[[-1, P]], channel_multiplier=1).then_inc(ident_ready, 1)
            for tile, value in CONSTANTS:
                nc.gpsimd.memset(tile[:], value).then_inc(consts_ready, 1)
            pool.wait_ge(adj_loaded, 16)
            for t in range(NT):
                nc.gpsimd.affine_select(out=adj_off[:, t], in_=adj_off[:, t], compare_op=ALU.not_equal, fill=0.0,
                                        base=t * P, pattern=[[-1, N]], channel_multiplier=1).then_inc(adj_ready, 1)

            def norms(p, b):
                done = upto(p, 6, 3 * b)
                pool.wait_ge(norm2_ready, upto(p, 2, b + 1))
                nc.gpsimd.tensor_tensor(rnorm[:, b], norm2[:, b], minus_half[:], ALU.pow).then_inc(pool_steps, 1)
                nc.gpsimd.tensor_tensor(norm[:, b], norm2[:, b], half[:], ALU.pow).then_inc(pool_steps, 1)
                pool.wait_ge(pool_steps, done + 1)
                for t in range(NT):
                    nc.gpsimd.tensor_tensor(r_wide[:, b, t], ones[:], rnorm[:, b, t:t + 1].broadcast_to([P, P]),
                                            ALU.mult).then_inc(r_ready, 1)
                pool.wait_ge(pool_steps, done + 2)
                nc.gpsimd.tensor_tensor(floor[:, b, L], norm[:, b], eps_row[:], ALU.mult).then_inc(pool_steps, 1)

            def layer_norm(q, b):
                done = upto(q, 6, 3 * b)
                pool.wait_ge(y_ready, upto(q, 4, 2 * b + 2))
                nc.gpsimd.tensor_tensor(minus_mean[:, b], row_sum[:, b], minus_one_by_d[:],
                                        ALU.mult).then_inc(mean_ready, 1)
                pool.wait_ge(sq_ready, upto(q, 4, 2 * b + 2))
                nc.gpsimd.tensor_tensor(msq[:, b], row_sq[:, b], one_by_d[:], ALU.mult).then_inc(ln_steps, 1)
                pool.wait_ge(ln_steps, done + 1)
                nc.gpsimd.tensor_tensor(var[:, b], msq[:, b], ln_eps_row[:], ALU.add).then_inc(ln_steps, 1)
                pool.wait_ge(ln_steps, done + 2)
                nc.gpsimd.tensor_tensor(rstd[:, b], var[:, b], minus_half[:], ALU.pow).then_inc(ln_steps, 1)
                pool.wait_ge(ln_steps, done + 3)
                nc.gpsimd.tensor_tensor(shift[:, b], minus_mean[:, b], rstd[:, b], ALU.mult).then_inc(ln_ready, 1)

            pool.wait_ge(consts_ready, len(CONSTANTS))
            for b in range(2):
                norms(0, b)

            def pair(p):
                for b in range(2):
                    layer_norm(p - 1, b)
                for b in range(2):
                    norms(p, b)

            with pool.Fori(1, PAIRS, 1) as p:
                pair(p)
            for b in range(2):
                layer_norm(PAIRS - 1, b)

        @block.scalar
        def _(act):
            load_w(act, L, w_lang, 1)

            def turn_hi(p, parity, b, k, bank=turn_bank):
                act.wait_ge(turned, upto(p, 4, 2 * b + k + 1))
                nc.scalar.copy(hT_hi[parity][:, 2 * k:2 * k + 2, b, :],
                               bank[:].rearrange("p (k n) -> p k n", k=2)).then_inc(hT_hi_ready, 1)

            def weight_hi(i, k):
                act.wait_ge(w_loaded[i][k // 2], 16)
                nc.scalar.copy(w_parts[i][0][:, k], raw[i][:, k]).then_inc(w_hi_ready, 1)

            def prep_hi_part(u):
                kind, g, i = prep_units[u]
                src = proj_bank[u % 3]
                if kind == MIRROR:
                    return
                act.wait_ge(prep_done, u + 1)
                if kind == UPPER:
                    nc.scalar.copy(m_hi[:, g, i, i * P:], src[:, i * P:])
                    nc.scalar.mul(md_hi[:, g, i], src[:, i * P:(i + 1) * P], 0.5).then_inc(prep_hi, 1)
                else:
                    dst = woT[0][:, i] if kind == WO_TURN else wvo_hi[:, i]
                    nc.scalar.copy(dst, src[:]).then_inc(prep_hi, 1)

            for k in range(DT):
                weight_hi(L, k)
            for u in range(PREP):
                if u == BEFORE_TURNS:
                    for b in range(2):
                        for k in range(2):
                            turn_hi(0, 0, b, k, first_bank(b, k))
                prep_hi_part(u)
                kind, g, i = prep_units[u]
                if kind == UPPER:
                    weight_hi((G, 2)[g], i)
            act.wait_ge(scal_loaded, 32)
            nc.scalar.activation(scal[:, 2:3], scal[:, 0:1], ACT.Exp, scale=-1.0).then_inc(scal_exp, 1)
            nc.scalar.activation(scal[:, 3:4], scal[:, 1:2], ACT.Exp).then_inc(scal_exp, 1)

            def proj_hi_part(p, k):
                act.wait_ge(proj_done, upto(p, PV, k + 1))
                src = proj_bank[k % 3]
                if k < 2 * DT:
                    dst = p_hi[:, :, k // 2, k % 2, :]
                    src = src[:].rearrange("p (b n) -> p b n", b=2)
                else:
                    b, t = divmod(k - 2 * DT, NT)
                    dst, src = v_hi[:, b, t], src[:]
                nc.scalar.copy(dst, src).then_inc(proj_hi, 1)

            def save_x(p, b, t):
                act.wait_ge(x_done, upto(p, 4, 2 * b + t + 1))
                nc.scalar.copy(xs[:, b, t], x_bank[t][:].rearrange("p (g n) -> p g n", g=2)).then_inc(x_saved, 1)

            def gauss(q, b):
                act.wait_ge(gram_ready, upto(q, 4, 2 * b + 2))
                nc.scalar.activation(wk(b, E), wk(b, SG), ACT.Exp, scale=scal[:, 6:7]).then_inc(exp_done, 1)

            def gauss_scaled(q, b):
                act.wait_ge(coef_steps, upto(q, 6, 3 * b + 3))
                for t in range(NT):
                    nc.scalar.activation(wk_t(b, GK)[:, t], wk_t(b, BG)[:, t], ACT.Copy,
                                         scale=coef[:, b, G, t:t + 1]).then_inc(gk_ready, 1)

            def kt_hi_part(q, b):
                act.wait_ge(kt_done, upto(q, 2, b + 1))
                nc.scalar.copy(kt_hi[:], gl_bank[:].rearrange("p (t n) -> p t n", t=NT)).then_inc(kt_hi_ready, 1)

            def squares(q, b):
                act.wait_ge(mean_ready, upto(q, 2, b + 1))
                for t in range(NT):
                    nc.scalar.activation(junk_a[:, t], y[:, b, t], ACT.Square, bias=minus_mean[:, b, t:t + 1],
                                         accum_out=row_sq[:, b, t:t + 1]).then_inc(sq_ready, 1)

            def normalise(q, b):
                act.wait_ge(ln_ready, upto(q, 2, b + 1))
                for t in range(NT):
                    nc.scalar.activation(y[:, b, t], y[:, b, t], ACT.Identity, bias=shift[:, b, t:t + 1],
                                         scale=rstd[:, b, t:t + 1]).then_inc(normed, 1)

            def pair(p, parity, first=False, last=False):
                q, tail = p - 1, not first
                proj_hi_part(p, 0)
                proj_hi_part(p, 1)
                if tail:
                    kt_hi_part(q, 0)
                proj_hi_part(p, 2)
                proj_hi_part(p, 3)
                if tail:
                    gauss(q, 1)
                proj_hi_part(p, 4)
                if tail:
                    squares(q, 0)
                proj_hi_part(p, 5)
                if tail:
                    gauss_scaled(q, 1)
                proj_hi_part(p, 6)
                if tail:
                    normalise(q, 0)
                proj_hi_part(p, 7)
                if tail:
                    kt_hi_part(q, 1)
                if last:
                    return
                proj_hi_part(p, 8)
                save_x(p, 0, 0)
                save_x(p, 0, 1)
                turn_hi(p + 1, 1 - parity, 0, 0)
                if tail:
                    squares(q, 1)
                proj_hi_part(p, 9)
                turn_hi(p + 1, 1 - parity, 0, 1)
                if tail:
                    normalise(q, 1)
                proj_hi_part(p, 10)
                turn_hi(p + 1, 1 - parity, 1, 0)
                gauss(p, 0)
                proj_hi_part(p, 11)
                turn_hi(p + 1, 1 - parity, 1, 1)
                save_x(p, 1, 0)
                gauss_scaled(p, 0)
                save_x(p, 1, 1)

            pair(0, 0, first=True)
            with act.Fori(0, LOOPS, 1) as i:
                pair(2 * i + 1, 1)
                pair(2 * i + 2, 0)
            p = PAIRS - 1
            pair(p, 1, last=True)
            save_x(p, 0, 0)
            save_x(p, 0, 1)
            squares(p - 1, 1)
            save_x(p, 1, 0)
            save_x(p, 1, 1)
            normalise(p - 1, 1)
            proj_hi_part(p, 8)
            gauss(p, 0)
            proj_hi_part(p, 9)
            proj_hi_part(p, 10)
            gauss_scaled(p, 0)
            proj_hi_part(p, 11)
            gauss(p, 1)
            kt_hi_part(p, 0)
            gauss_scaled(p, 1)
            kt_hi_part(p, 1)
            squares(p, 0)
            normalise(p, 0)
            squares(p, 1)
            normalise(p, 1)

        @block.vector
        def _(dve):
            def turn_lo(p, parity, b, k, bank=turn_bank):
                dve.wait_ge(hT_hi_ready, upto(p, 4, 2 * b + k + 1))
                nc.vector.tensor_tensor(hT_lo[parity][:, 2 * k:2 * k + 2, b, :],
                                        bank[:].rearrange("p (k n) -> p k n", k=2),
                                        hT_hi[parity][:, 2 * k:2 * k + 2, b, :].bitcast(F32),
                                        ALU.subtract).then_inc(hT_ready, 1)

            def weight_lo(i, k):
                dve.wait_ge(w_hi_ready, DT * i + k + 1)
                nc.vector.tensor_tensor(w_parts[i][1][:, k], raw[i][:, k], w_parts[i][0][:, k].bitcast(F32),
                                        ALU.subtract).then_inc(w_lo_ready, 1)

            def prep_lo_part(u):
                kind, g, i = prep_units[u]
                src = proj_bank[u % 3]
                a, e = i * P, (i + 1) * P
                if kind == MIRROR:
                    dve.wait_ge(prep_done, u + 1)
                    nc.vector.tensor_copy(m_hi[:, g, i, 0:a], src[:, 0:a]).then_inc(prep_lo, 1)
                    return
                dve.wait_ge(prep_hi, upto_unit(u))
                if kind == UPPER:
                    if e < D:
                        nc.vector.tensor_tensor(m_lo[:, g, i, e:], src[:, e:], m_hi[:, g, i, e:].bitcast(F32),
                                                ALU.subtract)
                    nc.vector.scalar_tensor_tensor(out=m_lo[:, g, i, a:e], in0=src[:, a:e], scalar=0.5,
                                                   in1=md_hi[:, g, i].bitcast(F32), op0=ALU.mult,
                                                   op1=ALU.subtract).then_inc(prep_lo, 1)
                else:
                    hi, lo = (woT[0][:, i], woT[1][:, i]) if kind == WO_TURN else (wvo_hi[:, i], wvo_lo[:, i])
                    nc.vector.tensor_tensor(lo, src[:], hi.bitcast(F32), ALU.subtract).then_inc(prep_lo, 1)

            for k in range(DT):
                weight_lo(L, k)
            for u in range(PREP):
                if u == BEFORE_TURNS:
                    for b in range(2):
                        for k in range(2):
                            turn_lo(0, 0, b, k, first_bank(b, k))
                prep_lo_part(u)
                kind, g, i = prep_units[u]
                if kind == UPPER:
                    weight_lo((G, 2)[g], i)
            dve.wait_ge(scal_exp, 2)
            nc.vector.tensor_scalar(scal[:, 4:5], scal[:, 2:3], 1.0, None, ALU.add).then_inc(scal_steps, 1)
            nc.vector.tensor_tensor(scal[:, 5:6], scal[:, 3:4], scal[:, 3:4], ALU.mult).then_inc(scal_steps, 1)
            dve.wait_ge(scal_steps, 2)
            nc.vector.reciprocal(scal[:, 7:8], scal[:, 4:5]).then_inc(scal_steps, 1)
            nc.vector.reciprocal(scal[:, 6:7], scal[:, 5:6]).then_inc(scal_steps, 1)
            dve.wait_ge(scal_steps, 4)
            for t in range(NT):
                nc.vector.tensor_copy(share[:, L, t:t + 1], scal[:, 7:8]).then_inc(scal_steps, 1)
                nc.vector.tensor_scalar(share[:, G, t:t + 1], scal[:, 7:8], -1.0, 1.0, ALU.mult,
                                        ALU.add).then_inc(scal_steps, 1)

            def proj_lo_part(p, k):
                dve.wait_ge(proj_hi, upto(p, PV, k + 1))
                src = proj_bank[k % 3]
                if k < 2 * DT:
                    hi, dst = p_hi[:, :, k // 2, k % 2, :], p_lo[:, :, k // 2, k % 2, :]
                    src = src[:].rearrange("p (b n) -> p b n", b=2)
                else:
                    b, t = divmod(k - 2 * DT, NT)
                    hi, dst, src = v_hi[:, b, t], v_lo[:, b, t], src[:]
                nc.vector.tensor_tensor(dst, src, hi.bitcast(F32), ALU.subtract).then_inc(proj_ready, 1)

            def diagonal(p, b):
                dve.wait_ge(x_saved, upto(p, 4, 2 * b + 2))
                for g in (G, L):
                    for t in range(NT):
                        ins = nc.vector.tensor_tensor_reduce(
                            out=junk_d[:, g, t], in0=xs[:, b, t, g, t * P:(t + 1) * P], in1=ident[:], scale=1.0,
                            scalar=0.0, op0=ALU.mult, op1=ALU.add, accum_out=x_diag[:, b, g, t:t + 1])
                ins.then_inc(diag_ready, 1)
                dve.wait_ge(diag_ready, upto(p, 2, b + 1))
                nc.vector.tensor_scalar(norm2[:, b], x_diag[:, b, L], 2.0, EPS * EPS, ALU.mult,
                                        ALU.max).then_inc(norm2_ready, 1)
                for t in range(NT):
                    nc.vector.tensor_scalar(xs[:, b, t, G], xs[:, b, t, G], x_diag[:, b, G, t:t + 1], None,
                                            ALU.subtract).then_inc(centred, 1)

            def gram(q, b, g):
                dve.wait_ge(gramT_done, upto(q, 4, 2 * b + g + 1))
                src = (gl_bank, gg_bank)[g]
                nc.vector.tensor_tensor(wk_t(b, (GL, SG)[g]), src[:].rearrange("p (t n) -> p t n", t=NT),
                                        xs[:, b, :, g], ALU.add).then_inc(gram_ready, 1)

            def gauss_masked(q, b):
                dve.wait_ge(exp_done, upto(q, 2, b + 1))
                for t in range(NT):
                    nc.vector.scalar_tensor_tensor(
                        out=wk_t(b, BG)[:, t], in0=wk_t(b, E)[:, t], scalar=1.0, in1=adj_off[:, t], op0=ALU.min,
                        op1=ALU.mult, accum_out=sums[:, b, G, t:t + 1]).then_inc(sums_ready, 1)

            def cosine_masked(q, b):
                dve.wait_ge(rcol_done, upto(q, 2, b + 1))
                nc.vector.tensor_tensor(wk_t(b, RADJ), gg_bank[:, 0:N].unsqueeze(1).broadcast_to([P, NT, N]),
                                        adj_off[:], ALU.mult).then_inc(radj_ready, 1)
                dve.wait_ge(radj_ready, upto(q, 2, b + 1))
                for t in range(NT):
                    nc.vector.scalar_tensor_tensor(
                        out=wk_t(b, BL)[:, t], in0=wk_t(b, GL)[:, t], scalar=0.0, in1=wk_t(b, RADJ)[:, t],
                        op0=ALU.max, op1=ALU.mult, accum_out=sums[:, b, L, t:t + 1]).then_inc(sums_ready, 1)

            def row_factors(q, b):
                done = upto(q, 6, 3 * b)
                dve.wait_ge(sums_ready, upto(q, 8, 4 * b + 4))
                dve.wait_ge(pool_steps, upto(q, 6, 3 * b + 3))
                nc.vector.tensor_tensor(den[:, b], sums[:, b], floor[:, b], ALU.max).then_inc(coef_steps, 1)
                dve.wait_ge(coef_steps, done + 1)
                nc.vector.reciprocal(rden[:, b], den[:, b]).then_inc(coef_steps, 1)
                dve.wait_ge(coef_steps, done + 2)
                nc.vector.tensor_tensor(coef[:, b], rden[:, b], share[:], ALU.mult).then_inc(coef_steps, 1)

            def kernel_sum(q, b):
                dve.wait_ge(coef_steps, upto(q, 6, 3 * b + 3))
                for t in range(NT):
                    dve.wait_ge(gk_ready, upto(q, 4, 2 * b + t + 1))
                    nc.vector.scalar_tensor_tensor(
                        out=wk_t(b, K)[:, t], in0=wk_t(b, BL)[:, t], scalar=coef[:, b, L, t:t + 1],
                        in1=wk_t(b, GK)[:, t], op0=ALU.mult, op1=ALU.add).then_inc(k_ready, 1)

            def kt_lo_part(q, b):
                dve.wait_ge(kt_hi_ready, upto(q, 2, b + 1))
                nc.vector.tensor_tensor(kt_lo[:], gl_bank[:].rearrange("p (t n) -> p t n", t=NT),
                                        kt_hi[:].bitcast(F32), ALU.subtract).then_inc(kt_ready, 1)

            def residual(q, parity, b, t, bank=turn_bank):
                dve.wait_ge(out_done, upto(q, 4, 2 * b + t + 1))
                if t == 0:
                    dve.wait_ge(y_moved[b], 16 * (q + 1))
                nc.vector.scalar_tensor_tensor(
                    out=y[:, b, t], in0=bank[:], scalar=1.0, in1=x_nat[parity][:, b, t], op0=ALU.mult,
                    op1=ALU.add, accum_out=row_sum[:, b, t:t + 1]).then_inc(y_ready, 1)

            def pair(p, parity, first=False, last=False):
                q, tail = p - 1, not first
                proj_lo_part(p, 0)
                proj_lo_part(p, 1)
                if tail:
                    kt_lo_part(q, 0)
                proj_lo_part(p, 2)
                proj_lo_part(p, 3)
                if tail:
                    gram(q, 1, L)
                    gram(q, 1, G)
                    residual(q, 1 - parity, 0, 0)
                proj_lo_part(p, 4)
                if tail:
                    gauss_masked(q, 1)
                    residual(q, 1 - parity, 0, 1)
                    cosine_masked(q, 1)
                    row_factors(q, 1)
                proj_lo_part(p, 5)
                if tail:
                    kernel_sum(q, 1)
                proj_lo_part(p, 6)
                proj_lo_part(p, 7)
                if tail:
                    kt_lo_part(q, 1)
                if last:
                    return
                proj_lo_part(p, 8)
                if tail:
                    residual(q, 1 - parity, 1, 0)
                    residual(q, 1 - parity, 1, 1)
                turn_lo(p + 1, 1 - parity, 0, 0)
                diagonal(p, 0)
                proj_lo_part(p, 9)
                turn_lo(p + 1, 1 - parity, 0, 1)
                proj_lo_part(p, 10)
                gram(p, 0, L)
                gram(p, 0, G)
                turn_lo(p + 1, 1 - parity, 1, 0)
                gauss_masked(p, 0)
                proj_lo_part(p, 11)
                turn_lo(p + 1, 1 - parity, 1, 1)
                cosine_masked(p, 0)
                row_factors(p, 0)
                kernel_sum(p, 0)
                diagonal(p, 1)

            dve.wait_ge(adj_ready, NT)
            dve.wait_ge(scal_steps, 8)
            pair(0, 0, first=True)
            with dve.Fori(0, LOOPS, 1) as i:
                pair(2 * i + 1, 1)
                pair(2 * i + 2, 0)
            p = PAIRS - 1
            pair(p, 1, last=True)
            residual(p - 1, 0, 1, 0)
            residual(p - 1, 0, 1, 1)
            diagonal(p, 0)
            diagonal(p, 1)
            proj_lo_part(p, 8)
            gram(p, 0, L)
            gram(p, 0, G)
            proj_lo_part(p, 9)
            gauss_masked(p, 0)
            cosine_masked(p, 0)
            row_factors(p, 0)
            proj_lo_part(p, 10)
            kernel_sum(p, 0)
            gram(p, 1, L)
            gram(p, 1, G)
            proj_lo_part(p, 11)
            gauss_masked(p, 1)
            kt_lo_part(p, 0)
            cosine_masked(p, 1)
            row_factors(p, 1)
            kernel_sum(p, 1)
            for b in range(2):
                if b == 1:
                    kt_lo_part(p, 1)
                for t in range(NT):
                    residual(p, 1, b, t, tail_bank(b, t))

        @block.tensor
        def _(pe):
            def products(dst, steps):
                for n, (lhsT, rhs) in enumerate(steps):
                    last = pe.matmul(dst, lhsT, rhs, start=(n == 0), stop=(n == len(steps) - 1))
                return last

            def turn(p, parity, b, k, first=False):
                n = upto(p, 4, 2 * b + k)
                if k == 0:
                    pe.wait_ge(x_loaded[parity][b], 8 * (p - parity) + 16)
                if b + k > 0 and not first:
                    pe.wait_ge(hT_ready, n)
                bank = first_bank(b, k) if first else turn_bank
                for kk in range(2):
                    for t in range(NT):
                        c = (2 * k + kk) * P
                        last = pe.transpose(bank[:, kk * N + t * P:kk * N + (t + 1) * P],
                                            x_nat[parity][:, b, t, c:c + P], ident[:])
                last.then_inc(turned, 1)

            def three_products(rows, stationary, moving, cols=slice(None)):
                (sh, sl), (mh, ml) = stationary, moving
                return [s for r in range(DT) for s in ((sh[:, r, rows], mh[:, r, cols]), (sh[:, r, rows], ml[:, r, cols]),
                                                       (sl[:, r, rows], mh[:, r, cols]))]

            def prepare(u):
                kind, g, i = prep_units[u]
                dst = proj_bank[u % 3]
                rows = slice(i * P, (i + 1) * P)
                if u >= 3:
                    pe.wait_ge(prep_lo, u - 2)
                if kind == UPPER:
                    cols = slice(i * P, D)
                    steps = three_products(rows, w_parts[g], w_parts[g], cols)
                    for n, (lhsT, rhs) in enumerate(steps):
                        if i == 0 and n % 3 == 0:
                            pe.wait_ge(w_lo_ready, DT * g + n // 3 + 1)
                        last = pe.matmul(dst[:, cols], lhsT, rhs, start=(n == 0), stop=(n == len(steps) - 1))
                elif kind == MIRROR:
                    pe.wait_ge(prep_lo, prepared(UPPER, g, i - 1))
                    for r in range(i):
                        last = pe.transpose(dst[:, r * P:(r + 1) * P], m_hi[:, g, r, rows].bitcast(F32), ident[:])
                elif kind == WO_TURN:
                    for b in range(2):
                        pe.wait_ge(y_moved[b], 16)
                    for r in range(DT):
                        last = pe.transpose(dst[:, r * P:(r + 1) * P], raw[3][:, r, rows], ident[:])
                else:
                    if i == 0:
                        pe.wait_ge(w_lo_ready, 3 * DT)
                        pe.wait_ge(prep_lo, prepared(WO_TURN, None, DT - 1))
                    last = products(dst[:], three_products(rows, w_parts[2], woT))
                last.then_inc(prep_done, 1)

            pe.wait_ge(ident_ready, 1)
            for u in range(BEFORE_TURNS):
                prepare(u)
            for b in range(2):
                for k in range(2):
                    turn(0, 0, b, k, first=True)
            for u in range(BEFORE_TURNS, PREP):
                prepare(u)

            def project(p, parity, k, first):
                j, g = divmod(k, 2)
                if k == 0:
                    pe.wait_ge(hT_ready, upto(p, 4, 4))
                if not (first and k < 3):
                    pe.wait_ge(proj_ready, upto(p, PV, k - 2))
                elif k == 0:
                    pe.wait_ge(prep_lo, PREP)
                hi = [hT_hi[parity][:, i].rearrange("p b n -> p (b n)") for i in range(DT)]
                lo = [hT_lo[parity][:, i].rearrange("p b n -> p (b n)") for i in range(DT)]
                c = slice(j * P, (j + 1) * P)
                steps = []
                for i in range(DT):
                    steps.append((m_hi[:, g, i, c], lo[i]))
                    if i <= j:
                        steps.append((m_hi[:, g, i, c] if i < j else md_hi[:, g, i], hi[i]))
                        steps.append((m_lo[:, g, i, c], hi[i]))
                products(proj_bank[k % 3][:], steps).then_inc(proj_done, 1)

            def value(p, parity, b, t):
                k = 2 * DT + NT * b + t
                pe.wait_ge(proj_ready, upto(p, PV, k - 2))
                rows = slice(t * P, (t + 1) * P)
                steps = []
                for i in range(DT):
                    hi, lo = hT_hi[parity][:, i, b, rows], hT_lo[parity][:, i, b, rows]
                    steps += [(hi, wvo_hi[:, i]), (hi, wvo_lo[:, i]), (lo, wvo_hi[:, i])]
                products(proj_bank[k % 3][:], steps).then_inc(proj_done, 1)

            def x_tile(p, parity, b, t):
                n = upto(p, 4, 2 * b + t)
                if b == 0 and t == 0:
                    pe.wait_ge(proj_ready, upto(p, PV, 2 * DT))
                if not (type(n) is int and n < 2):
                    pe.wait_ge(x_saved, n - 1)
                steps = []
                for i in range(DT):
                    lhsT = hT_hi[parity][:, i, b, t * P:(t + 1) * P]
                    steps += [(lhsT, part[:, b, i].rearrange("p g n -> p (g n)")) for part in (p_hi, p_lo)]
                products(x_bank[t][:], steps).then_inc(x_done, 1)

            def gram_turn(q, b, g):
                if g == L:
                    pe.wait_ge(x_saved, upto(q, 4, 2 * b + 2))
                else:
                    pe.wait_ge(centred, upto(q, 4, 2 * b + 2))
                dst = (gl_bank, gg_bank)[g]
                for t in range(NT):
                    for u in range(NT):
                        last = pe.transpose(dst[:, t * N + u * P:t * N + (u + 1) * P],
                                            xs[:, b, u, g, t * P:(t + 1) * P], ident[:])
                last.then_inc(gramT_done, 1)

            def r_turn(q, b):
                pe.wait_ge(r_ready, upto(q, 4, 2 * b + 2))
                pe.wait_ge(gram_ready, upto(q, 4, 2 * b + 2))
                for t in range(NT):
                    last = pe.transpose(gg_bank[:, t * P:(t + 1) * P], r_wide[:, b, t], ident[:])
                last.then_inc(rcol_done, 1)

            def k_turn(q, b):
                pe.wait_ge(k_ready, upto(q, 4, 2 * b + 2))
                for u in range(NT):
                    for t in range(NT):
                        last = pe.transpose(gl_bank[:, u * N + t * P:u * N + (t + 1) * P],
                                            wk_t(b, K)[:, t, u * P:(u + 1) * P], ident[:])
                last.then_inc(kt_done, 1)

            def k_times_v(q, b, t, bank_free, count, bank=turn_bank):
                if t == 0:
                    pe.wait_ge(kt_ready, upto(q, 2, b + 1))
                pe.wait_ge(bank_free, count)
                steps = []
                for u in range(NT):
                    hi, lo = kt_hi[:, u, t * P:(t + 1) * P], kt_lo[:, u, t * P:(t + 1) * P]
                    steps += [(hi, v_hi[:, b, u]), (hi, v_lo[:, b, u]), (lo, v_hi[:, b, u])]
                products(bank[:], steps).then_inc(out_done, 1)

            def pair(p, parity, first=False, last=False):
                q, tail = p - 1, not first
                project(p, parity, 0, first)
                project(p, parity, 1, first)
                if tail:
                    k_turn(q, 0)
                project(p, parity, 2, first)
                project(p, parity, 3, first)
                if tail:
                    k_times_v(q, 0, 0, hT_ready, upto(p, 4, 4))
                    gram_turn(q, 1, L)
                    gram_turn(q, 1, G)
                project(p, parity, 4, first)
                if tail:
                    k_times_v(q, 0, 1, y_ready, upto(q, 4, 1))
                    r_turn(q, 1)
                project(p, parity, 5, first)
                project(p, parity, 6, first)
                project(p, parity, 7, first)
                if tail:
                    k_turn(q, 1)
                if last:
                    return
                value(p, parity, 0, 0)
                if tail:
                    k_times_v(q, 1, 0, y_ready, upto(q, 4, 2))
                x_tile(p, parity, 0, 0)
                if tail:
                    k_times_v(q, 1, 1, y_ready, upto(q, 4, 3))
                x_tile(p, parity, 0, 1)
                if tail:
                    pe.wait_ge(y_ready, upto(q, 4, 4))
                turn(p + 1, 1 - parity, 0, 0)
                value(p, parity, 0, 1)
                turn(p + 1, 1 - parity, 0, 1)
                value(p, parity, 1, 0)
                gram_turn(p, 0, L)
                gram_turn(p, 0, G)
                turn(p + 1, 1 - parity, 1, 0)
                value(p, parity, 1, 1)
                r_turn(p, 0)
                turn(p + 1, 1 - parity, 1, 1)
                x_tile(p, parity, 1, 0)
                x_tile(p, parity, 1, 1)

            pair(0, 0, first=True)
            with pe.Fori(0, LOOPS, 1) as i:
                pair(2 * i + 1, 1)
                pair(2 * i + 2, 0)
            p = PAIRS - 1
            pair(p, 1, last=True)
            x_tile(p, 1, 0, 0)
            k_times_v(p - 1, 1, 0, y_ready, upto(p - 1, 4, 2))
            x_tile(p, 1, 0, 1)
            k_times_v(p - 1, 1, 1, y_ready, upto(p - 1, 4, 3))
            x_tile(p, 1, 1, 0)
            x_tile(p, 1, 1, 1)
            value(p, 1, 0, 0)
            gram_turn(p, 0, L)
            gram_turn(p, 0, G)
            value(p, 1, 0, 1)
            r_turn(p, 0)
            value(p, 1, 1, 0)
            pe.wait_ge(gram_ready, upto(p, 4, 1))
            gram_turn(p, 1, L)
            pe.wait_ge(radj_ready, upto(p, 2, 1))
            gram_turn(p, 1, G)
            value(p, 1, 1, 1)
            pe.wait_ge(gram_ready, upto(p, 4, 3))
            k_turn(p, 0)
            r_turn(p, 1)
            pe.wait_ge(proj_ready, upto(p, PV, PV))
            for b in range(2):
                if b == 1:
                    k_turn(p, 1)
                for t in range(NT):
                    k_times_v(p, b, t, y_ready, upto(p, 4, 0), tail_bank(b, t))


_INS = ['x', 'adj', 'L0_gnn_W_lang', 'L0_gnn_W_grav', 'L0_gnn_W_V', 'L0_gnn_W_O', 'L0_gnn_gate_logit',
        'L0_gnn_log_sigma']


def kernel(**inputs):
    import numpy as _np
    import concourse.bacc as _bacc
    from concourse.bass_utils import run_bass_kernel_spmd as _run

    nc = _bacc.Bacc("TRN2", target_bir_lowering=False, num_devices=1)
    arrays, args = {}, []
    for name in _INS:
        a = _np.ascontiguousarray(inputs[name])
        arrays[f"in_{name}"] = a
        args.append(nc.dram_tensor(f"in_{name}", a.shape, mybir.dt.from_np(a.dtype), kind="ExternalInput").ap())
    out = nc.dram_tensor("out_y", arrays["in_x"].shape, F32, kind="ExternalOutput").ap()
    gnn_resnorm(nc, *args, out)
    r = _run(nc, [arrays], core_ids=[0])
    return r.results[0]["out_y"]
```
